# Optimizing a Trainium2 kernel written in Bass

```python
import numpy as np
import jax
import jax.numpy as jnp

def _softmax(x, axis=-1):
    return jax.nn.softmax(x, axis=axis)
def _gelu(x):
    return jax.nn.gelu(x, approximate=True)
def _silu(x):
    return jax.nn.silu(x)
def _sigmoid(x):
    return jax.nn.sigmoid(x)
def _layernorm(x, axis=-1, eps=1e-5):
    m = jnp.mean(x, axis=axis, keepdims=True)
    v = jnp.var(x, axis=axis, keepdims=True)
    return (x - m) / jnp.sqrt(v + eps)
def _scatter_add(tgt, idx, src, axis=0):
    return tgt.at[idx].add(src)
def _segment_sum(src, seg, n):
    return jax.ops.segment_sum(src, seg, n)

kernel_name = 'mk_conv_preact_d1_conv_nhwc768_8fdda3'

def setup_inputs(seed: int = 0):
    np.random.seed(seed)
    _w = jnp.asarray
    def _rec_inputs():
        import jax
        import jax.numpy as jnp
        _gk = jax.random.key(seed)
        x = 7.572e-06 + 1 * jax.random.normal(jax.random.fold_in(_gk, 1), (64, 14, 14, 768), jnp.float32)
        return x
    x = _rec_inputs()
    def _L0_conv_setup():
        import jax, jax.numpy as jnp
        import numpy as np
        B, H, W = (64, 14, 14)
        DIM, NH, LORA = (768, 12, 4)
        HD = DIM // NH
        key = jax.random.key(seed)
        ks = jax.random.split(key, 12)
        s = 0.02
        return {'x': jax.random.normal(ks[0], (B, H, W, DIM), dtype=jnp.float32), 'qkv_w': jax.random.normal(ks[1], (3 * DIM, DIM), dtype=jnp.float32) * s, 'qkv_b': jax.random.normal(ks[2], (3 * DIM,), dtype=jnp.float32) * s, 'proj_w': jax.random.normal(ks[3], (DIM, DIM), dtype=jnp.float32) * s, 'proj_b': jax.random.normal(ks[4], (DIM,), dtype=jnp.float32) * s, 'la_q': jax.random.normal(ks[5], (LORA, DIM), dtype=jnp.float32) * s, 'lb_q': jax.random.normal(ks[6], (DIM, LORA), dtype=jnp.float32) * s, 'la_v': jax.random.normal(ks[7], (LORA, DIM), dtype=jnp.float32) * s, 'lb_v': jax.random.normal(ks[8], (DIM, LORA), dtype=jnp.float32) * s, 'rel_pos_h': jax.random.normal(ks[9], (2 * H - 1, HD), dtype=jnp.float32) * s, 'rel_pos_w': jax.random.normal(ks[10], (2 * W - 1, HD), dtype=jnp.float32) * s}
    _L0_conv_all = _L0_conv_setup()
    _L0_conv_in = {k: v for k, v in _L0_conv_all.items() if k in ('qkv_w', 'qkv_b', 'proj_w', 'proj_b', 'la_q', 'lb_q', 'la_v', 'lb_v', 'rel_pos_h', 'rel_pos_w', )}
    del _L0_conv_all

    return {
        "x": x,
        "L0_conv_qkv_w": _L0_conv_in["qkv_w"],
        "L0_conv_qkv_b": _L0_conv_in["qkv_b"],
        "L0_conv_proj_w": _L0_conv_in["proj_w"],
        "L0_conv_proj_b": _L0_conv_in["proj_b"],
        "L0_conv_la_q": _L0_conv_in["la_q"],
        "L0_conv_lb_q": _L0_conv_in["lb_q"],
        "L0_conv_la_v": _L0_conv_in["la_v"],
        "L0_conv_lb_v": _L0_conv_in["lb_v"],
        "L0_conv_rel_pos_h": _L0_conv_in["rel_pos_h"],
        "L0_conv_rel_pos_w": _L0_conv_in["rel_pos_w"],
    }

def reference(x, L0_conv_qkv_w, L0_conv_qkv_b, L0_conv_proj_w, L0_conv_proj_b, L0_conv_la_q, L0_conv_lb_q, L0_conv_la_v, L0_conv_lb_v, L0_conv_rel_pos_h, L0_conv_rel_pos_w):
    import jax
    import jax.numpy as jnp
    def _L0_conv_ref(x, qkv_w, qkv_b, proj_w, proj_b, la_q, lb_q, la_v, lb_v, rel_pos_h, rel_pos_w):
        import jax, jax.numpy as jnp
        import numpy as np
        B, H, W = (64, 14, 14)
        DIM, NH, LORA = (768, 12, 4)
        HD = DIM // NH
        b, h, w, c = x.shape
        nh, hd = (NH, c // NH)
        scale = hd ** (-0.5)
        qkv = x @ qkv_w.T + qkv_b
        new_q = x @ la_q.T @ lb_q.T
        new_v = x @ la_v.T @ lb_v.T
        qkv = qkv.at[..., :c].add(new_q)
        qkv = qkv.at[..., 2 * c:].add(new_v)
        qkv = qkv.reshape(b, h * w, 3, nh, hd).transpose(2, 0, 3, 1, 4)
        qkv = qkv.reshape(3, b * nh, h * w, hd)
        q, k, v = (qkv[0], qkv[1], qkv[2])
        attn = jnp.einsum('bqd,bkd->bqk', q * scale, k)
        idx_h = jnp.arange(h)[:, None] - jnp.arange(h)[None, :] + (h - 1)
        idx_w = jnp.arange(w)[:, None] - jnp.arange(w)[None, :] + (w - 1)
        Rh = rel_pos_h[idx_h]
        Rw = rel_pos_w[idx_w]
        r_q = q.reshape(b * nh, h, w, hd)
        rel_h = jnp.einsum('bhwc,hkc->bhwk', r_q, Rh)
        rel_w = jnp.einsum('bhwc,wkc->bhwk', r_q, Rw)
        attn = (attn.reshape(b * nh, h, w, h, w) + rel_h[:, :, :, :, None] + rel_w[:, :, :, None, :]).reshape(b * nh, h * w, h * w)
        attn = jax.nn.softmax(attn, axis=-1)
        out = jnp.einsum('bqk,bkd->bqd', attn, v)
        out = out.reshape(b, nh, h, w, hd).transpose(0, 2, 3, 1, 4).reshape(b, h, w, c)
        return out @ proj_w.T + proj_b

    def _gn(v, G=32, eps=1e-5):
        B_, H_, W_, C_ = v.shape
        g = v.reshape(B_, H_, W_, G, C_ // G)
        m = jnp.mean(g, axis=(1, 2, 4), keepdims=True)
        s = jnp.var(g, axis=(1, 2, 4), keepdims=True)
        return ((g - m) / jnp.sqrt(s + eps)).reshape(v.shape)

    def _ln_c(v, eps=1e-6):
        m = jnp.mean(v, axis=-1, keepdims=True)
        s = jnp.var(v, axis=-1, keepdims=True)
        return (v - m) / jnp.sqrt(s + eps)

    def _ln_t(v, eps=1e-5):
        m = jnp.mean(v, axis=-1, keepdims=True)
        s = jnp.var(v, axis=-1, keepdims=True)
        return (v - m) / jnp.sqrt(s + eps)

    def _to_tokens(v):
        B_, H_, W_, C_ = v.shape
        return v.reshape(B_, H_ * W_, C_)
    def _from_tokens(t, like):
        return t.reshape(like.shape)

    x = x + _L0_conv_ref(_gn(x), L0_conv_qkv_w, L0_conv_qkv_b, L0_conv_proj_w, L0_conv_proj_b, L0_conv_la_q, L0_conv_lb_q, L0_conv_la_v, L0_conv_lb_v, L0_conv_rel_pos_h, L0_conv_rel_pos_w)
    return x


_drawn_inputs = setup_inputs


def setup_inputs(seed=0):
    import zlib

    import numpy as np

    out = dict(_drawn_inputs(seed))
    spreads = {}
    factors = {'L0_conv_qkv_b': 5.121,
     'L0_conv_proj_b': 2.778,
     'L0_conv_la_q': 8.0,
     'L0_conv_lb_q': 8.0,
     'L0_conv_la_v': 8.0,
     'L0_conv_lb_v': 8.0,
     'L0_conv_rel_pos_h': 8.0,
     'L0_conv_rel_pos_w': 8.0}
    for name, (base, spread) in spreads.items():
        noise = np.random.default_rng([zlib.crc32(name.encode()), seed]).standard_normal(out[name].shape)
        drawn = base * np.exp(spread * noise) if base else spread * noise
        out[name] = jnp.asarray(drawn.astype(out[name].dtype))
    for name, factor in factors.items():
        out[name] = (out[name] * factor).astype(out[name].dtype)
    return out
```

```python
from contextlib import ExitStack

import concourse.bass as bass
from concourse import mybir

F32 = mybir.dt.float32
F16 = mybir.dt.float16
U32 = mybir.dt.uint32
ALU = mybir.AluOpType
ACT = mybir.ActivationFunctionType
AX = mybir.AxisListType
RMAX = bass.bass_isa.ReduceOp.max

B, H, W, C = 64, 14, 14, 768
NH, HD = 12, 64
LORA = 4
GROUPS = 32
EPS = 1e-5
PAIRS = B // 2
TOK = H * W
HALF = TOK // 2
NT = 2 * TOK
CT = C // 128
HP = NH // 2
GP = C // GROUPS // CT
SW = H * 2 * HP
RC = 3
RCH = (H + RC - 1) // RC
REL_ONE = 4096.0
REL_EXP = float(8.0 / REL_ONE)
SCALE = HD ** -0.5

PHASE1 = [("Q", 0, 0), ("S", 1, 5, 1), ("T", 1, 5, 0), ("N", 1, 5, 1), ("P", 1, 4, 1),
          ("Q", 0, 1), ("Q", 0, 2), ("P", 1, 5, 0), ("T", 1, 5, 1), ("Q", 0, 3), ("P", 1, 5, 1), ("Q", 0, 4),
          ("Q", 0, 5), ("Y", 1, 0), ("R", 0, 0), ("Y", 1, 1), ("Z", 1, 0), ("R", 0, 1),
          ("Y", 1, 2), ("Z", 1, 1), ("R", 0, 2), ("Y", 1, 3), ("Z", 1, 2), ("R", 0, 3), ("R", 0, 4),
          ("K", 0, 0), ("Z", 1, 3), ("Y", 1, 4), ("Y", 1, 5), ("Z", 1, 4),
          ("S", 0, 0, 0), ("N", 0, 0, 0), ("V", 0, 0), ("Z", 1, 5), ("VX", 0, 0)]
NEXT = {
    "pe": [("", "X0 X1", "", "X2"), ("", "X3 X4", "", "X5"), ("", "G0", "", "G1"), ("", "", "", ""), ("", "", "", "")],
    "act": [("", "X0 X1", "", "X2"), ("", "X3 X4", "", "X5"), ("", "", "", "G1"), ("", "H0", "", ""),
            ("H1", "H2", "", "")],
    "dve": [("", "", "X0 X1", "X2"), ("", "", "X3 X4", "X5 M0"), ("", "G0", "", "G1"), ("H0", "", "H1", ""),
            ("H2", "", "", "")],
}


def phase2(engine):
    out = []
    for hp in range(1, HP):
        h = hp - 1
        next_pair = [[(s[0], -1, int(s[1])) for s in part.split()] for part in NEXT[engine][h]]
        big, scores = ("K", 0, hp), ("S", 0, h, 1)
        out += [scores, big] if engine == "dve" else [big, scores]
        out += [("T", 0, h, 0), ("N", 0, h, 1)] + next_pair[0]
        if h:
            out.append(("P", 0, h - 1, 1))
        out += [("V", 0, hp)] + next_pair[1] + [("S", 0, hp, 0), ("T", 0, h, 1), ("N", 0, hp, 0)] + next_pair[2]
        out += [("P", 0, h, 0), ("VX", 0, hp)] + next_pair[3]
    return out


MIDDLE = PHASE1 + phase2("pe")
ACT_ORDER = PHASE1 + phase2("act")
DVE_ORDER = [PHASE1[1], PHASE1[0]] + PHASE1[2:] + phase2("dve")
RING_KINDS = ("Q", "K", "V", "VX", "R", "Y", "Z", "X", "G")
RING_STEPS = [s for s in MIDDLE if s[0] in RING_KINDS]
PER_PAIR = {"Q": 6, "K": 6, "V": 6, "VX": 6, "R": RCH, "Y": 6, "Z": 6, "X": 6, "G": 2}


def ring_bank(step):
    n = RING_STEPS.index(step)
    return (n + (n >= RING_STEPS.index(("Q", 0, 2))) + (n >= RING_STEPS.index(("Q", 0, 4)))) % 3


def ring_before(order, before, n):
    bank = ring_bank(order[n])
    for s in reversed(order[:n]):
        if s[0] in RING_KINDS and ring_bank(s) == bank:
            return s, 0
    for s in reversed(before):
        if s[0] in RING_KINDS and ring_bank(s) == bank:
            return s, 1
    return None, 0


class Turn:

    def __init__(self, q, par, half):
        self.q, self.par, self.half = q, par, half

    def of(self, old):
        if old == 0:
            return self
        if self.par == 0:
            return Turn(self.q - old, 1, self.half - (1 if old == 1 else 0))
        return Turn(self.q - old, 0, self.half + (1 if old == -1 else 0))


def wait(eng, sem, per, q, k):
    if isinstance(q, int):
        if per * q + k > 0:
            eng.wait_ge(sem, per * q + k)
    else:
        eng.wait_ge(sem, q * per + k)


def walk(eng, steps, middle, loop_pairs):
    first = [s for s in middle if s[1] != 1]
    last = [s for s in middle if s[1] != -1]
    lead = [s for s in middle if s[1] == -1]
    tail = [s for s in middle if s[1] == 1]
    steps("lead", lead, [], Turn(-1, 1, -1))
    steps("first", first, lead, Turn(0, 0, 0))
    with eng.Fori(0, loop_pairs // 2) as it:
        steps("loop", middle, middle, Turn(it * 2 + 1, 1, it))
        steps("loop", middle, middle, Turn(it * 2 + 2, 0, it + 1))
    n = loop_pairs + 1
    steps("last", last, middle, Turn(n, n % 2, n // 2))
    steps("tail", tail, last, Turn(n + 1, (n + 1) % 2, (n + 1) // 2))


def build(nc, x, qkv_w, qkv_b, proj_w, proj_b, la_q, lb_q, la_v, lb_v, rel_h, rel_w, out, pairs=PAIRS):
    V, A, T, G = nc.vector, nc.scalar, nc.tensor, nc.gpsimd
    with ExitStack() as keep:
        def sb(stack, name, shape, dt):
            return stack.enter_context(nc.sbuf_tensor(name, shape, dt))

        w_hi = sb(keep, "w_hi", [128, CT, 4 * C], F16)
        w_lo = sb(keep, "w_lo", [128, CT, 4 * C], F16)
        rt_hi = sb(keep, "rt_hi", [128, 2, H, 64], F16)
        rt_lo = sb(keep, "rt_lo", [128, 2, H, 64], F16)
        k_one = sb(keep, "k_one", [128, 2, 2, NT], F16)
        k_two = sb(keep, "k_two", [128, 2, 2, NT], F16)
        ident = sb(keep, "ident", [128, 128], F32)
        gmean = sb(keep, "gmean", [128, 128], F32)
        bias = sb(keep, "bias", [128, 24], F32)
        pw = sb(keep, "pw", [128, 5], F32)
        inv = sb(keep, "inv", [128, 5], F32)
        exp_scale = sb(keep, "exp_scale", [128, 1], F32)
        neg_scale = sb(keep, "neg_scale", [128, 1], F32)
        rel_scale = sb(keep, "rel_scale", [128, 1], F32)
        rel_hi_scale = sb(keep, "rel_hi_scale", [128, 1], F32)
        y_scale = sb(keep, "y_scale", [128, 1], F32)

        x_sb = sb(keep, "x_sb", [HALF, 2, 4, C], F32)
        x_in = [keep.enter_context(nc.semaphore(f"x_in{i}")) for i in range(2)]
        x_rows = x.rearrange("(n b) h w c -> (n b h w) c", b=2).rearrange("(n t p) c -> n p t c", t=4, p=HALF)

        prepare(nc, locals())
        attend(nc, locals(), pairs)
    return nc


def prepare(nc, g):
    V, A, T, G, sb = g["V"], g["A"], g["T"], g["G"], g["sb"]
    w_hi, w_lo, rt_hi, rt_lo, k_one = g["w_hi"], g["w_lo"], g["rt_hi"], g["rt_lo"], g["k_one"]
    ident, gmean, bias, pw, inv = g["ident"], g["gmean"], g["bias"], g["pw"], g["inv"]
    NR = 2 * H - 1
    with ExitStack() as own:
        stage = sb(own, "stage", [128, 24, C], F32)
        la = sb(own, "la", [LORA, 2, C], F32)
        lbT = sb(own, "lbT", [LORA, 2, C], F32)
        rel = sb(own, "rel", [NR, 2, 2, HD], F32)
        pick = sb(own, "pick", [NR, H, H], F32)
        rel16 = sb(own, "rel16", [128, 2, 2, TOK], F16)
        onehot = sb(own, "onehot", [128, TOK], F16)
        mx = sb(own, "mx", [128, 5], F32)
        bmx = sb(own, "bmx", [128, 4], F32)
        tile_mx = sb(own, "tile_mx", [128, 2 * CT], F32)
        top = sb(own, "top", [128, 5], F32)
        expo = sb(own, "expo", [128, 5], U32)
        tmp = sb(own, "tmp", [128, 1], F32)
        mask = sb(own, "mask", [128, 1], F32)
        ring = own.enter_context(nc.psum_tensor("prep_ring", [128, 4, 512], F32))
        lora_ps = own.enter_context(nc.psum_tensor("lora_ps", [128, 4, 512], F32))
        sem = lambda name: own.enter_context(nc.semaphore(name))
        w_in = [sem(f"w_in{i}") for i in range(4)]
        lora_in, small_in = sem("lora_in"), sem("small_in")
        merged, lora_done = sem("merged"), sem("lora_done")
        pool_step, consts_made, maxima, reduced, scaled = (
            sem("pool_step"), sem("consts_made"), sem("maxima"), sem("reduced"), sem("scaled"))
        dve_step = sem("dve_step")
        turned, hi_made, lo_made = sem("turned"), sem("hi_made"), sem("lo_made")
        rel_ps_done, rel_hi_made, rel_lo_made = sem("rel_ps_done"), sem("rel_hi_made"), sem("rel_lo_made")
        turns = [(grp, t, CT * grp + j) for grp in range(4) for t in range(CT) for j in (0, 3)]
        lora_tiles = list(range(0, CT)) + list(range(2 * CT, 3 * CT))
        block = own.enter_context(nc.Block())

        @block.sync
        def _(sp):
            sp.dma_start(la[:, 0, :], g["la_q"]).then_inc(lora_in, 16)
            sp.dma_start(la[:, 1, :], g["la_v"]).then_inc(lora_in, 16)
            sp.dma_start(lbT[:, 0, :], g["lb_q"].rearrange("c r -> r c"),
                         allow_slow_non_contiguous=True).then_inc(lora_in, 16)
            sp.dma_start(lbT[:, 1, :], g["lb_v"].rearrange("c r -> r c"),
                         allow_slow_non_contiguous=True).then_inc(lora_in, 16)
            for i, src in ((0, g["qkv_w"][0:C]), (1, g["qkv_w"][C:2 * C]), (3, g["proj_w"]),
                           (2, g["qkv_w"][2 * C:3 * C])):
                sp.dma_start(stage[:, CT * i:CT * i + CT, :],
                             src.rearrange("(j p) c -> p j c", p=128)).then_inc(w_in[i], 16)
            sp.dma_start(g["x_sb"][:, 0], g["x_rows"][0]).then_inc(g["x_in"][0], 16)

        @block.scalar
        def _(act):
            act.dma_start(bias[:, 0:18], g["qkv_b"].rearrange("(j p) -> p j", p=128),
                          allow_slow_non_contiguous=True).then_inc(small_in, 16)
            act.dma_start(bias[:, 18:24], g["proj_b"].rearrange("(j p) -> p j", p=128),
                          allow_slow_non_contiguous=True).then_inc(small_in, 16)
            for copy in range(2):
                act.dma_start(rel[:, 0, copy, :], g["rel_h"]).then_inc(small_in, 16)
                act.dma_start(rel[:, 1, copy, :], g["rel_w"]).then_inc(small_in, 16)
            act.wait_ge(scaled, 1)
            for n, (grp, t, j0) in enumerate(turns):
                act.wait_ge(turned, n + 1)
                A.activation(w_hi[:, t, 128 * j0:128 * j0 + 384], ring[:, n % 4, 0:384], ACT.Copy,
                             scale=inv[:, grp:grp + 1]).then_inc(hi_made, 1)
            act.wait_ge(rel_ps_done, 1)
            for ax in range(2):
                A.activation(rel16[:, 0, ax, :], lora_ps[:, ax, 0:TOK], ACT.Copy,
                             scale=inv[:, 4:5]).then_inc(rel_hi_made, 1)

        @block.gpsimd
        def _(pool):
            count = [0]

            def step(ins):
                count[0] += 1
                ins.then_inc(pool_step, 1)
                pool.wait_ge(pool_step, count[0])

            step(G.memset(ident[:, :], 0.0))
            step(G.affine_select(out=ident[:, :], in_=ident[:, :], compare_op=ALU.not_equal, fill=1.0, base=0,
                                 pattern=[[-1, 128]], channel_multiplier=1))
            step(G.memset(gmean[:, :], 1.0 / GP))
            view = gmean[:, :].rearrange("p (a b) -> p a b", b=GP)
            step(G.affine_select(out=view, in_=view, compare_op=ALU.is_ge, fill=0.0, base=0,
                                 pattern=[[-GP, 128 // GP], [0, GP]], channel_multiplier=1))
            step(G.affine_select(out=view, in_=view, compare_op=ALU.is_ge, fill=0.0, base=GP - 1,
                                 pattern=[[GP, 128 // GP], [0, GP]], channel_multiplier=-1))
            step(G.memset(pick[:, :, :], 0.0))
            step(G.affine_select(out=pick[:, :, :], in_=pick[:, :, :], compare_op=ALU.not_equal, fill=1.0,
                                 base=1 - H, pattern=[[-1, H], [1, H]], channel_multiplier=1))
            step(G.memset(onehot[:, :], 0.0))
            for quad in range(4):
                view = onehot[:, :].rearrange("p (h w) -> p h w", h=H)
                pattern = [[-1, H], [0, W]] if quad % 2 == 0 else [[0, H], [-1, W]]
                for part in range(2):
                    step(G.affine_select(out=view, in_=view, compare_op=ALU.not_equal, fill=REL_ONE,
                                         base=-(32 * quad + 16 * part), pattern=pattern, channel_multiplier=1))
            step(G.memset(mask[:, :], 0.0))
            for at in range(16, 128, 16):
                step(G.affine_select(out=mask[:, :], in_=mask[:, :], compare_op=ALU.is_ge,
                                     fill=float(at // 16 % 2), base=at - 1, pattern=[[0, 1]],
                                     channel_multiplier=-1))
            G.memset(mx[:, :], 0.0).then_inc(consts_made, 1)
            pool.wait_ge(maxima, 1)
            G.partition_all_reduce(top[:, :], mx[:, :], 128, RMAX).then_inc(reduced, 1)
            pool.wait_ge(reduced, 1)
            for slot in range(2):
                for image in range(2):
                    keys = slice(TOK * image, TOK * image + TOK)
                    step(G.tensor_copy(k_one[64:128, slot, 0, keys], onehot[64:128, :]))
                    step(G.tensor_copy(k_one[0:64, slot, 1, keys], onehot[0:64, :]))

        @block.vector
        def _(dve):
            count = [0]

            def step(ins):
                count[0] += 1
                ins.then_inc(dve_step, 1)
                dve.wait_ge(dve_step, count[0])

            V.memset(expo[:, :], 0x7F800000)
            V.memset(rt_hi[:, :, :, :], 0.0)
            step(V.memset(rt_lo[:, :, :, :], 0.0))
            dve.wait_ge(consts_made, 1)

            def maximum(i):
                V.tensor_reduce(mx[:, i:i + 1], stage[:, CT * i:CT * i + CT, :], AX.XY, ALU.max,
                                apply_absolute_value=True)

            for n, j in enumerate(lora_tiles):
                if n == CT:
                    dve.wait_ge(w_in[1], 16)
                    maximum(1)
                    dve.wait_ge(w_in[3], 16)
                    maximum(3)
                dve.wait_ge(w_in[j // CT], 16)
                dve.wait_ge(lora_done, n + 1)
                V.tensor_tensor(stage[:, j, :].rearrange("p (a c) -> p a c", a=2),
                                stage[:, j, :].rearrange("p (a c) -> p a c", a=2),
                                lora_ps[:, 2 * (n % 2):2 * (n % 2) + 2, 0:384], ALU.add).then_inc(merged, 1)
                dve.wait_ge(merged, n + 1)
                V.tensor_reduce(tile_mx[:, n:n + 1], stage[:, j, :], AX.X, ALU.max, apply_absolute_value=True)
            dve.wait_ge(small_in, 16 * 6)
            step(V.memset(tmp[:, :], 0.0))
            V.tensor_reduce(mx[:, 0:1], tile_mx[:, 0:CT], AX.X, ALU.max)
            V.tensor_reduce(mx[:, 2:3], tile_mx[:, CT:2 * CT], AX.X, ALU.max)
            for i in range(4):
                V.tensor_reduce(bmx[:, i:i + 1], bias[:, CT * i:CT * i + CT], AX.X, ALU.max,
                                apply_absolute_value=True)
            step(V.tensor_reduce(mx[0:NR, 4:5], rel[:, :, 0, :], AX.XY, ALU.max, apply_absolute_value=True))
            step(V.tensor_tensor(mx[:, 0:3], mx[:, 0:3], bmx[:, 0:3], ALU.max))
            V.tensor_scalar(mx[:, :], mx[:, :], 1e-30, None, ALU.max).then_inc(maxima, 1)
            dve.wait_ge(reduced, 1)
            step(V.tensor_tensor(pw[:, :].bitcast(U32), top[:, :].bitcast(U32), expo[:, :], ALU.bitwise_and))
            step(V.tensor_scalar(tmp[:, :], pw[:, 4:5], 0.125, None, ALU.mult))
            step(V.tensor_tensor(pw[:, 1:2], pw[:, 1:2], tmp[:, :], ALU.max))
            step(V.reciprocal(inv[:, :], pw[:, :]))
            for i in range(3):
                step(V.tensor_scalar(bias[:, CT * i:CT * i + CT], bias[:, CT * i:CT * i + CT],
                                     inv[:, i:i + 1], None, ALU.mult))
            step(V.scalar_tensor_tensor(g["exp_scale"][:, :], pw[:, 0:1], SCALE, pw[:, 1:2], ALU.mult, ALU.mult))
            step(V.tensor_scalar(g["neg_scale"][:, :], g["exp_scale"][:, :], -1.0, None, ALU.mult))
            step(V.scalar_tensor_tensor(g["rel_scale"][:, :], pw[:, 4:5], REL_EXP, inv[:, 1:2], ALU.mult, ALU.mult))
            step(V.tensor_tensor(g["rel_hi_scale"][:, :], g["rel_scale"][:, :], mask[:, :], ALU.mult))
            step(V.tensor_tensor(g["y_scale"][:, :], pw[:, 3:4], pw[:, 2:3], ALU.mult))
            V.tensor_copy(tmp[:, :], pw[:, 0:1]).then_inc(scaled, 1)
            for n, (grp, t, j0) in enumerate(turns):
                dve.wait_ge(hi_made, n + 1)
                V.scalar_tensor_tensor(w_lo[:, t, 128 * j0:128 * j0 + 384], ring[:, n % 4, 0:384],
                                       inv[:, grp:grp + 1], w_hi[:, t, 128 * j0:128 * j0 + 384],
                                       ALU.mult, ALU.subtract).then_inc(lo_made, 1)
            for ax in range(2):
                dve.wait_ge(rel_hi_made, ax + 1)
                V.scalar_tensor_tensor(rel16[:, 1, ax, :], lora_ps[:, ax, 0:TOK], inv[:, 4:5],
                                       rel16[:, 0, ax, :], ALU.mult, ALU.subtract).then_inc(rel_lo_made, 1)
            dve.wait_ge(rel_lo_made, 2)
            for part, table in enumerate((rt_hi, rt_lo)):
                for head in range(2):
                    for at in (32 * head, 32 * head + 16):
                        rows = slice(64 * head, 64 * head + 64)
                        V.tensor_copy(table[rows, :, :, at:at + H],
                                      rel16[rows, part, :, :].rearrange("p a (r k) -> p a r k", r=H))

        @block.tensor
        def _(pe):
            pe.wait_ge(lora_in, 16 * 4)
            for n, j in enumerate(lora_tiles):
                if n >= 2:
                    pe.wait_ge(merged, n - 1)
                which, jj = n // CT, n % CT
                for half in range(2):
                    last = T.matmul(lora_ps[:, 2 * (n % 2) + half, 0:384],
                                    lbT[:, which, 128 * jj:128 * jj + 128],
                                    la[:, which, 384 * half:384 * half + 384], start=True, stop=True)
                last.then_inc(lora_done, 1)
            pe.wait_ge(merged, 12)
            pe.wait_ge(small_in, 16 * 6)
            pe.wait_ge(pool_step, 7)
            for ax in range(2):
                last = T.matmul(lora_ps[:, ax, 0:TOK], rel[:, ax, :, :].rearrange("r c d -> r (c d)"),
                                pick[:, :, :].rearrange("r a b -> r (a b)"), start=True, stop=True)
            last.then_inc(rel_ps_done, 1)
            pe.wait_ge(w_in[1], 16)
            pe.wait_ge(w_in[3], 16)
            for n, (grp, t, j0) in enumerate(turns):
                if n >= 4:
                    pe.wait_ge(lo_made, n - 3)
                for i in range(3):
                    if grp < 3:
                        src = stage[:, j0 + i, :].rearrange("p (a b) -> p b a", b=CT)[:, t, :]
                    else:
                        src = stage[:, j0 + i, 128 * t:128 * t + 128]
                    last = T.transpose(ring[:, n % 4, 128 * i:128 * i + 128], src, ident[:, :])
                last.then_inc(turned, 1)


def attend(nc, g, pairs):
    V, A, T, G, sb = g["V"], g["A"], g["T"], g["G"], g["sb"]
    w_hi, w_lo, rt_hi, rt_lo = g["w_hi"], g["w_lo"], g["rt_hi"], g["rt_lo"]
    k_one, k_two = g["k_one"], g["k_two"]
    ident, gmean, bias = g["ident"], g["gmean"], g["bias"]
    exp_scale, neg_scale, rel_scale, rel_hi_scale, y_scale = (
        g["exp_scale"], g["neg_scale"], g["rel_scale"], g["rel_hi_scale"], g["y_scale"])
    x_sb, x_in, x_rows = g["x_sb"], g["x_in"], g["x_rows"]
    out_rows = g["out"].rearrange("(n b) h w c -> (n b h w) c", b=2).rearrange("(n t p) c -> n p t c", t=4, p=HALF)
    with ExitStack() as own:
        S = lambda name, shape, dt: sb(own, name, shape, dt)
        sem = lambda name: own.enter_context(nc.semaphore(name))
        xT = S("xT", [128, CT, NT], F32)
        xn_hi = S("xn_hi", [128, 2, CT, NT], F16)
        xn_lo = S("xn_lo", [128, 2, CT, NT], F16)
        q_one = S("q_one", [128, 2, HP, NT], F16)
        q_two = S("q_two", [128, 2, HP, NT], F16)
        rel_sb = S("rel_sb", [128, HP, NT], F16)
        rel_part = S("rel_part", [128, 2, RC * SW], F16)
        vT = S("vT", [128, 2, NT], F32)
        v_hi = S("v_hi", [HALF, 2, 4, 128], F16)
        v_lo = S("v_lo", [HALF, 2, 4, 128], F16)
        prob = S("prob", [HALF, 2, 2, 2, TOK], F32)
        pT_hi = S("pT_hi", [HALF, 2, 2, 2 * TOK], F16)
        pT_lo = S("pT_lo", [HALF, 2, 2, 2 * TOK], F16)
        o_hi = S("o_hi", [128, HP, NT], F16)
        o_lo = S("o_lo", [128, HP, NT], F16)
        yT = S("yT", [128, 2, NT], F32)
        y_sb = S("y_sb", [HALF, 2, 4, 128], F32)
        row_max = S("row_max", [HALF, 2, 4], F32)
        neg_max = S("neg_max", [HALF, 2, 4], F32)
        row_sum = S("row_sum", [HALF, 2, 4], F32)
        row_inv = S("row_inv", [HALF, 2, 4], F32)
        stats = S("stats", [128, 2, CT, 6], F32)
        mean_var = S("mean_var", [128, 2, 2], F32)
        mean = S("mean", [128, 2], F32)
        spread = S("spread", [128, 2], F32)
        var_eps = S("var_eps", [128, 2], F32)
        rstd = S("rstd", [128, 2], F32)
        minus_half = S("minus_half", [128, 2], F32)
        ring = own.enter_context(nc.psum_tensor("ring", [128, 3, 512], F32))
        score = own.enter_context(nc.psum_tensor("score", [128, 2, 512], F32))
        pT = own.enter_context(nc.psum_tensor("pT", [128, 2, 512], F32))
        o_ps = own.enter_context(nc.psum_tensor("o_ps", [128, 512], F32))

        y_out = [sem("y_out0"), sem("y_out1")]
        q_copied, rel_copied, k_copied = sem("q_copied"), sem("rel_copied"), sem("k_copied")
        y_sb_free = sem("y_sb_free")
        done = {k: sem(f"done_{k}") for k in RING_KINDS}
        read = {k: sem(f"read_{k}") for k in RING_KINDS}
        hi_made = {k: sem(f"hi_made_{k}") for k in ("Q", "K", "VX", "R")}
        scores_done, neg_max_made, exps_done, probs_ready = (
            sem("scores_done"), sem("neg_max_made"), sem("exps_done"), sem("probs_ready"))
        pT_done, pT_hi_made, pT_lo_made = sem("pT_done"), sem("pT_hi_made"), sem("pT_lo_made")
        pv_done, o_hi_made, o_lo_made = sem("pv_done"), sem("o_hi_made"), sem("o_lo_made")
        row_max_made, row_inv_made = sem("row_max_made"), sem("row_inv_made")
        minus_half_made = sem("minus_half_made")
        stats_made, dev_made, rstd_made = sem("stats_made"), sem("dev_made"), sem("rstd_made")
        group_in, normed, xn_hi_made, xn_lo_made = sem("group_in"), sem("normed"), sem("xn_hi_made"), sem("xn_lo_made")
        block = own.enter_context(nc.Block())

        @block.sync
        def _(sp):
            def load(turn):
                q = turn.q
                if not (isinstance(q, int) and q < 2):
                    wait(sp, read["Z"], 6, q - 2, 6)
                sp.dma_start(x_sb[:, turn.par], x_rows[q]).then_inc(x_in[turn.par], 16)

            def store(turn, m):
                wait(sp, read["Z"], 6, turn.q, m + 1)
                sp.dma_start(out_rows[turn.q][:, :, 128 * m:128 * m + 128],
                             y_sb[:, m % 2]).then_inc(y_out[m % 2], 16)

            def copy_q_hi(turn):
                wait(sp, hi_made["Q"], 6, turn.q, 6)
                sp.dma_start(q_two[64:128, 0], q_one[0:64, 0]).then_inc(q_copied, 16)
                sp.dma_start(q_two[0:64, 1], q_one[64:128, 1]).then_inc(q_copied, 16)

            def copy_rel(turn):
                wait(sp, read["R"], RCH, turn.q, RCH)
                for head in range(2):
                    for ax in range(2):
                        at = 64 * (1 - head) + 32 * ax
                        sp.dma_start(q_one[at:at + 32, head],
                                     rel_sb[64 * ax + 32 * head:64 * ax + 32 * head + 32]).then_inc(rel_copied, 16)

            def copy_k_hi(turn, k):
                wait(sp, hi_made["K"], 6, turn.q, k + 1)
                for head in range(2):
                    rows = slice(64 * head, 64 * head + 64)
                    sp.dma_start(k_two[rows, k % 2, head], k_one[rows, k % 2, head]).then_inc(k_copied, 16)

            def steps(phase, order, before, turn):
                if phase not in ("lead", "tail"):
                    copy_q_hi(turn)
                if phase not in ("lead", "first"):
                    for m in range(3):
                        store(turn.of(1), m)
                if phase not in ("lead", "tail"):
                    copy_rel(turn)
                    copy_k_hi(turn, 0)
                if phase not in ("lead", "first"):
                    for m in range(3, 6):
                        store(turn.of(1), m)
                if phase not in ("lead", "last", "tail"):
                    load(turn.of(-1))
                if phase not in ("lead", "tail"):
                    if phase != "first":
                        for slot in range(2):
                            wait(sp, y_out[slot], 48, turn.q, 0)
                    sp.sem_inc(y_sb_free, 1)
                    for k in range(1, HP):
                        copy_k_hi(turn, k)

            walk(sp, steps, MIDDLE, pairs - 2)
            for slot in range(2):
                sp.wait_ge(y_out[slot], 16 * 3 * pairs)

        @block.tensor
        def _(pe):
            def steps(phase, order, before, turn):
                for n, step in enumerate(order):
                    kind, old, k = step[:3]
                    t = turn.of(old)
                    if kind in RING_KINDS:
                        bank = ring_bank(step)
                        s, ago = ring_before(order, before, n)
                        if s is not None:
                            wait(pe, read[s[0]], PER_PAIR[s[0]], turn.q - ago - s[1], s[2] + 1)
                    if kind in ("Q", "K", "V"):
                        j = CT * "QKV".index(kind) + k
                        for c in range(CT):
                            if kind == "Q" and k == 0 and c % 2 == 0:
                                wait(pe, xn_lo_made, 3, t.q, c // 2 + 1)
                            for part, (w, xx) in enumerate(((w_hi, xn_hi), (w_hi, xn_lo), (w_lo, xn_hi))):
                                last = T.matmul(ring[:, bank, 0:NT], w[:, c, 128 * j:128 * j + 128],
                                                xx[:, t.par, c, :], start=(c == 0 and part == 0),
                                                stop=(c == CT - 1 and part == 2))
                        last.then_inc(done[kind], 1)
                    elif kind == "VX":
                        wait(pe, read["V"], 6, t.q, k + 1)
                        for i in range(4):
                            last = T.transpose(ring[0:HALF, bank, 128 * i:128 * i + 128],
                                               vT[:, k % 2, HALF * i:HALF * i + HALF], ident[:, :])
                        last.then_inc(done[kind], 1)
                    elif kind == "R":
                        if k == 0:
                            wait(pe, read["Q"], 6, t.q, 6)
                        T.matmul(ring[:, bank, 0:2], w_hi[:, 0, 0:128], w_hi[:, 0, 0:2], start=True, stop=True)
                        for i, row in enumerate(range(RC * k, min(RC * k + RC, H))):
                            for part, (tab, qq) in enumerate(((rt_hi, q_one), (rt_hi, q_two), (rt_lo, q_one))):
                                for ax in range(2):
                                    for head in range(2):
                                        rows = slice(64 * head, 64 * head + 64)
                                        to = slice(64 * ax + 32 * head, 64 * ax + 32 * head + 32)
                                        grid = qq[rows, head].rearrange("p a (b h w) -> p (a b) h w", b=2, h=H)
                                        mov = grid[:, :, row, :] if ax == 0 else grid[:, :, :, row]
                                        last = T.matmul(ring[to, bank, SW * i:SW * i + SW],
                                                        tab[rows, ax, row, 32 * head:32 * head + 32], mov,
                                                        start=(part == 0), stop=(part == 2))
                        last.then_inc(done[kind], 1)
                    elif kind == "S":
                        unit = 2 * k + step[3]
                        if unit == 0:
                            wait(pe, q_copied, 32, t.q, 32)
                            wait(pe, rel_copied, 64, t.q, 64)
                        wait(pe, read["K"], 6, t.q, k + 1)
                        wait(pe, k_copied, 192, t.q, 32 * k + 32)
                        wait(pe, exps_done, 12, t.q, unit)
                        c0 = TOK * step[3]
                        keys = slice(c0, c0 + TOK)
                        for half in range(2):
                            qs = slice(c0 + HALF * half, c0 + HALF * half + HALF)
                            to = slice(TOK * half, TOK * half + TOK)
                            for part, (qq, kk) in enumerate(((q_one, k_one), (q_two, k_two))):
                                for head in range(2):
                                    last = T.matmul(score[0:HALF, head, to], qq[:, head, k, qs],
                                                    kk[:, k % 2, head, keys], start=(part == 0), stop=(part == 1))
                        last.then_inc(scores_done, 1)
                    elif kind == "T":
                        unit = 2 * k + step[3]
                        wait(pe, probs_ready, 12, t.q, unit + 1)
                        wait(pe, pT_lo_made, 12, t.q, unit)
                        for head in range(2):
                            for kh in range(2):
                                for half in range(2):
                                    at = TOK * kh + HALF * half
                                    last = T.transpose(pT[0:HALF, head, at:at + HALF],
                                                       prob[:, step[3], head, half, HALF * kh:HALF * kh + HALF],
                                                       ident[0:HALF, 0:HALF])
                        last.then_inc(pT_done, 1)
                    elif kind == "P":
                        unit = 2 * k + step[3]
                        wait(pe, pT_lo_made, 12, t.q, unit + 1)
                        wait(pe, read["VX"], 6, t.q, k + 1)
                        if step[3] == 0:
                            wait(pe, o_lo_made, 6, t.q, k)
                        c0 = TOK * step[3]
                        for kh in range(2):
                            for part, (vv, pp) in enumerate(((v_hi, pT_hi), (v_hi, pT_lo), (v_lo, pT_hi))):
                                for head in range(2):
                                    rows = slice(64 * head, 64 * head + 64)
                                    last = T.matmul(o_ps[rows, c0:c0 + TOK], vv[:, k % 2, 2 * step[3] + kh, rows],
                                                    pp[:, step[3], head, TOK * kh:TOK * kh + TOK],
                                                    start=(kh == 0 and part == 0), stop=(kh == 1 and part == 2))
                        last.then_inc(pv_done, 1)
                    elif kind == "Y":
                        if k == 0:
                            wait(pe, o_lo_made, 6, t.q, 6)
                        j = 3 * CT + k
                        for c in range(HP):
                            for part, (w, oo) in enumerate(((w_hi, o_hi), (w_hi, o_lo), (w_lo, o_hi))):
                                last = T.matmul(ring[:, bank, 0:NT], w[:, c, 128 * j:128 * j + 128], oo[:, c, :],
                                                start=(c == 0 and part == 0), stop=(c == HP - 1 and part == 2))
                        last.then_inc(done[kind], 1)
                    elif kind == "Z":
                        wait(pe, read["Y"], 6, t.q, k + 1)
                        for i in range(4):
                            last = T.transpose(ring[0:HALF, bank, 128 * i:128 * i + 128],
                                               yT[:, k % 2, HALF * i:HALF * i + HALF], ident[:, :])
                        last.then_inc(done[kind], 1)
                    elif kind == "X":
                        if k == 0:
                            wait(pe, x_in[t.par], 16, t.half, 16)
                        for i in range(4):
                            src = x_sb[:, t.par, i, :].rearrange("p (a b) -> p b a", b=CT)[:, k, :]
                            last = T.transpose(ring[:, bank, HALF * i:HALF * i + HALF], src, ident[0:HALF, 0:HALF])
                        last.then_inc(done[kind], 1)
                    elif kind == "G":
                        wait(pe, group_in, 2, t.q, k + 1)
                        src = mean_var[:, :, 0] if k == 0 else spread[:, :]
                        T.matmul(ring[:, bank, 0:2], gmean[:, :], src, start=True, stop=True).then_inc(done[kind], 1)

            walk(pe, steps, MIDDLE, pairs - 2)

        @block.scalar
        def _(act):
            def steps(phase, order, before, turn):
                for step in order:
                    kind, old, k = step[:3]
                    t = turn.of(old)
                    bank = ring_bank(step) if kind in RING_KINDS else 0
                    if kind in ("Q", "K"):
                        wait(act, done[kind], 6, t.q, k + 1)
                        j = CT * "QK".index(kind) + k
                        for head in range(2):
                            rows = slice(64 * head, 64 * head + 64)
                            to = q_one[rows, head, k, :] if kind == "Q" else k_one[rows, k % 2, head, :]
                            last = A.activation(to, ring[rows, bank, 0:NT], ACT.Identity, bias=bias[rows, j:j + 1])
                        last.then_inc(hi_made[kind], 1)
                    elif kind == "V":
                        wait(act, done[kind], 6, t.q, k + 1)
                        A.activation(vT[:, k % 2, :], ring[:, bank, 0:NT], ACT.Copy).then_inc(read["V"], 1)
                    elif kind == "VX":
                        wait(act, done[kind], 6, t.q, k + 1)
                        if not (phase == "first" and k < 2):
                            wait(act, pv_done, 12, t.q, 2 * k - 2)
                        A.activation(v_hi[:, k % 2].rearrange("p a b -> p (a b)"), ring[0:HALF, bank, :],
                                     ACT.Copy).then_inc(hi_made[kind], 1)
                    elif kind == "R":
                        wait(act, done[kind], RCH, t.q, k + 1)
                        wait(act, read["R"], RCH, t.q, max(k - 1, 0))
                        n = SW * min(RC, H - RC * k)
                        A.activation(rel_part[:, k % 2, 0:n], ring[:, bank, 0:n], ACT.Copy,
                                     scale=rel_hi_scale[:, :]).then_inc(hi_made[kind], 1)
                    elif kind == "N":
                        unit = 2 * k + step[3]
                        wait(act, neg_max_made, 12, t.q, unit + 1)
                        for i in range(4):
                            head, half = i // 2, i % 2
                            last = A.activation(prob[:, step[3], head, half, :],
                                                score[0:HALF, head, TOK * half:TOK * half + TOK], ACT.Exp,
                                                bias=neg_max[:, step[3], i:i + 1], scale=exp_scale[0:HALF, :],
                                                accum_out=row_sum[:, step[3], i:i + 1])
                        last.then_inc(exps_done, 1)
                    elif kind == "T":
                        unit = 2 * k + step[3]
                        wait(act, pT_done, 12, t.q, unit + 1)
                        if not (phase == "first" and unit < 2):
                            wait(act, pv_done, 12, t.q, unit - 1)
                        A.activation(pT_hi[:, step[3]], pT[0:HALF, :, 0:2 * TOK], ACT.Copy).then_inc(pT_hi_made, 1)
                    elif kind == "P" and step[3] == 1:
                        wait(act, pv_done, 12, t.q, 2 * k + 2)
                        A.activation(o_hi[:, k, :], o_ps[:, 0:NT], ACT.Identity,
                                     bias=bias[:, 2 * CT + k:2 * CT + k + 1]).then_inc(o_hi_made, 1)
                    elif kind == "Y":
                        wait(act, done[kind], 6, t.q, k + 1)
                        if k >= 2:
                            wait(act, done["Z"], 6, t.q, k - 1)
                        A.activation(yT[:, k % 2, :], ring[:, bank, 0:NT], ACT.Identity,
                                     bias=bias[:, 3 * CT + k:3 * CT + k + 1],
                                     scale=y_scale[:, :]).then_inc(read["Y"], 1)
                    elif kind == "X":
                        wait(act, done[kind], 6, t.q, k + 1)
                        if k == 0:
                            wait(act, xn_lo_made, 3, t.q, 0)
                        A.activation(xT[:, k, :], ring[:, bank, 0:NT], ACT.Copy).then_inc(read["X"], 1)
                    elif kind == "H":
                        wait(act, normed, 3, t.q, k + 1)
                        two = slice(2 * k, 2 * k + 2)
                        A.activation(xn_hi[:, t.par, two], xT[:, two, :], ACT.Copy).then_inc(xn_hi_made, 1)

            walk(act, steps, ACT_ORDER, pairs - 2)

        @block.gpsimd
        def _(pool):
            def steps(phase, order, before, turn):
                for step in order:
                    if step[0] == "G" and step[2] == 1:
                        t = turn.of(step[1])
                        wait(pool, read["G"], 2, t.q, 2)
                        G.tensor_tensor(rstd[:, :], var_eps[:, :], minus_half[:, :], ALU.pow).then_inc(rstd_made, 1)
                    elif step[0] == "H":
                        t = turn.of(step[1])
                        wait(pool, xn_hi_made, 3, t.q, step[2] + 1)
                        two = slice(2 * step[2], 2 * step[2] + 2)
                        G.tensor_tensor(xn_lo[:, t.par, two], xT[:, two, :], xn_hi[:, t.par, two],
                                        ALU.subtract).then_inc(xn_lo_made, 1)

            G.memset(minus_half[:, :], -0.5).then_inc(minus_half_made, 1)
            pool.wait_ge(minus_half_made, 1)
            walk(pool, steps, ACT_ORDER, pairs - 2)

        @block.vector
        def _(dve):
            def steps(phase, order, before, turn):
                for n, step in enumerate(order):
                    kind, old, k = step[:3]
                    t = turn.of(old)
                    bank = ring_bank(step) if kind in RING_KINDS else 0
                    if kind in ("Q", "K"):
                        wait(dve, hi_made[kind], 6, t.q, k + 1)
                        j = CT * "QK".index(kind) + k
                        for head in range(2):
                            rows = slice(64 * head, 64 * head + 64)
                            other = slice(64 - 64 * head, 128 - 64 * head)
                            if kind == "Q":
                                hi, lo = q_one[rows, head, k, :], q_two[rows, head, k, :]
                            else:
                                hi, lo = k_one[rows, k % 2, head, :], k_two[other, k % 2, head, :]
                            last = V.scalar_tensor_tensor(lo, ring[rows, bank, 0:NT], bias[rows, j:j + 1], hi,
                                                          ALU.add, ALU.subtract)
                        last.then_inc(read[kind], 1)
                    elif kind == "VX":
                        wait(dve, hi_made[kind], 6, t.q, k + 1)
                        V.tensor_tensor(v_lo[:, k % 2].rearrange("p a b -> p (a b)"), ring[0:HALF, bank, :],
                                        v_hi[:, k % 2].rearrange("p a b -> p (a b)"),
                                        ALU.subtract).then_inc(read[kind], 1)
                    elif kind == "R":
                        wait(dve, hi_made[kind], RCH, t.q, k + 1)
                        n_rows = min(RC, H - RC * k)
                        for ax in range(2):
                            rows = slice(64 * ax, 64 * ax + 64)
                            grid = rel_sb[rows, :, :].rearrange("p a (b h w) -> p (a b) h w", b=2, h=H)
                            for i in range(n_rows):
                                line = RC * k + i
                                to = grid[:, :, line, :] if ax == 0 else grid[:, :, :, line]
                                cols = slice(SW * i, SW * i + SW)
                                last = V.scalar_tensor_tensor(
                                    to, ring[rows, bank, cols].rearrange("p (g w) -> p g w", w=W),
                                    rel_scale[rows, :],
                                    rel_part[rows, k % 2, cols].rearrange("p (g w) -> p g w", w=W),
                                    ALU.mult, ALU.subtract)
                        last.then_inc(read[kind], 1)
                    elif kind == "S":
                        unit = 2 * k + step[3]
                        wait(dve, scores_done, 12, t.q, unit + 1)
                        V.tensor_reduce(row_max[:, step[3], :],
                                        score[0:HALF, :, 0:2 * TOK].rearrange("p a (b k) -> p a b k", b=2),
                                        AX.X, ALU.max).then_inc(row_max_made, 1)
                        wait(dve, row_max_made, 12, t.q, unit + 1)
                        V.tensor_scalar(neg_max[:, step[3], :], row_max[:, step[3], :], neg_scale[0:HALF, :], None,
                                        ALU.mult).then_inc(neg_max_made, 1)
                    elif kind == "N":
                        unit = 2 * k + step[3]
                        wait(dve, exps_done, 12, t.q, unit + 1)
                        V.reciprocal(row_inv[:, step[3], :], row_sum[:, step[3], :]).then_inc(row_inv_made, 1)
                        wait(dve, row_inv_made, 12, t.q, unit + 1)
                        for i in range(4):
                            pr = prob[:, step[3], i // 2, i % 2, :]
                            last = V.tensor_scalar(pr, pr, row_inv[:, step[3], i:i + 1], None, ALU.mult)
                        last.then_inc(probs_ready, 1)
                    elif kind == "T":
                        unit = 2 * k + step[3]
                        wait(dve, pT_hi_made, 12, t.q, unit + 1)
                        V.tensor_tensor(pT_lo[:, step[3]], pT[0:HALF, :, 0:2 * TOK], pT_hi[:, step[3]],
                                        ALU.subtract).then_inc(pT_lo_made, 1)
                    elif kind == "P" and step[3] == 1:
                        wait(dve, o_hi_made, 6, t.q, k + 1)
                        V.scalar_tensor_tensor(o_lo[:, k, :], o_ps[:, 0:NT], bias[:, 2 * CT + k:2 * CT + k + 1],
                                               o_hi[:, k, :], ALU.add, ALU.subtract).then_inc(o_lo_made, 1)
                    elif kind == "Z":
                        wait(dve, done[kind], 6, t.q, k + 1)
                        if k >= 2:
                            wait(dve, y_out[k % 2], 48, t.q, 16 * (k // 2))
                        else:
                            wait(dve, y_sb_free, 1, t.q, 1)
                        V.tensor_tensor(y_sb[:, k % 2], ring[0:HALF, bank, :].rearrange("p (a b) -> p a b", a=4),
                                        x_sb[:, t.par, :, 128 * k:128 * k + 128], ALU.add).then_inc(read["Z"], 1)
                    elif kind == "X":
                        wait(dve, read["X"], 6, t.q, k + 1)
                        for image in range(2):
                            V.bn_stats(stats[:, image, k, :],
                                       xT[:, k, TOK * image:TOK * image + TOK]).then_inc(stats_made, 1)
                    elif kind == "M":
                        wait(dve, stats_made, 12, t.q, 12)
                        V.memset(spread[:, :], 0.0)
                        V.bn_aggr(mean_var[:, 0, :], stats[:, 0].rearrange("p a b -> p (a b)"))
                        V.bn_aggr(mean_var[:, 1, :], stats[:, 1].rearrange("p a b -> p (a b)")).then_inc(group_in, 1)
                    elif kind == "G" and k == 0:
                        wait(dve, done["G"], 2, t.q, 1)
                        V.tensor_copy(mean[:, :], ring[:, bank, 0:2]).then_inc(read["G"], 1)
                        wait(dve, read["G"], 2, t.q, 1)
                        V.tensor_tensor(spread[:, :], mean_var[:, :, 0], mean[:, :], ALU.subtract).then_inc(dev_made, 1)
                        wait(dve, dev_made, 2, t.q, 1)
                        V.tensor_tensor(spread[:, :], spread[:, :], spread[:, :], ALU.mult).then_inc(dev_made, 1)
                        wait(dve, dev_made, 2, t.q, 2)
                        V.tensor_tensor(spread[:, :], spread[:, :], mean_var[:, :, 1], ALU.add).then_inc(group_in, 1)
                    elif kind == "G":
                        wait(dve, done["G"], 2, t.q, 2)
                        V.tensor_scalar(var_eps[:, :], ring[:, bank, 0:2], EPS, None, ALU.add).then_inc(read["G"], 1)
                    elif kind == "H":
                        if k == 0:
                            wait(dve, rstd_made, 1, t.q, 1)
                        for image in range(2):
                            part = xT[:, 2 * k:2 * k + 2, TOK * image:TOK * image + TOK]
                            last = V.tensor_scalar(part, part, mean[:, image:image + 1], rstd[:, image:image + 1],
                                                   ALU.subtract, ALU.mult)
                        last.then_inc(normed, 1)

            walk(dve, steps, DVE_ORDER, pairs - 2)


_INS = ["x", "L0_conv_qkv_w", "L0_conv_qkv_b", "L0_conv_proj_w", "L0_conv_proj_b", "L0_conv_la_q",
        "L0_conv_lb_q", "L0_conv_la_v", "L0_conv_lb_v", "L0_conv_rel_pos_h", "L0_conv_rel_pos_w"]


def kernel(**inputs):
    import numpy as np
    import concourse.bacc as bacc
    from concourse.bass_utils import run_bass_kernel_spmd

    nc = bacc.Bacc("TRN2", target_bir_lowering=False, num_devices=1)
    arrays, args = {}, []
    for name in _INS:
        a = np.ascontiguousarray(inputs[name])
        arrays[f"in_{name}"] = a
        args.append(nc.dram_tensor(f"in_{name}", a.shape, mybir.dt.from_np(a.dtype), kind="ExternalInput").ap())
    args.append(nc.dram_tensor("out_0", (B, H, W, C), F32, kind="ExternalOutput").ap())
    build(nc, *args)
    r = run_bass_kernel_spmd(nc, [arrays], core_ids=[0])
    return r.results[0]["out_0"]
```
